# Optimizing a Trainium2 kernel written in Bass

```python
import numpy as np
import jax
import jax.numpy as jnp

def _softmax(x, axis=-1):
    return jax.nn.softmax(x, axis=axis)

def _gelu(x):
    return jax.nn.gelu(x, approximate=True)

def _silu(x):
    return jax.nn.silu(x)

def _sigmoid(x):
    return jax.nn.sigmoid(x)

def _layernorm(x, axis=-1, eps=1e-05):
    m = jnp.mean(x, axis=axis, keepdims=True)
    v = jnp.var(x, axis=axis, keepdims=True)
    return (x - m) / jnp.sqrt(v + eps)

def _scatter_add(tgt, idx, src, axis=0):
    return tgt.at[idx].add(src)

def _segment_sum(src, seg, n):
    return jax.ops.segment_sum(src, seg, n)
kernel_name = 'mk_conv_seq_d1_conv_nhwc256_r4_55cb96'

def setup_inputs(seed: int=0):
    np.random.seed(seed)
    _w = jnp.asarray

    def _rec_inputs():
        import jax
        import jax.numpy as jnp
        _gk = jax.random.key(seed)
        x = 7.22e-05 + 1 * jax.random.normal(jax.random.fold_in(_gk, 1), (8, 16, 16, 64), jnp.float32)
        return x
    x = _rec_inputs()

    def _L0_conv_setup():
        import jax, jax.numpy as jnp
        import numpy as np

        def _l2n(v, eps=1e-12):
            return v / (jnp.linalg.norm(v) + eps)

        def _sn(W, u):
            v = _l2n(W.T @ u)
            u_new = _l2n(W @ v)
            v = jax.lax.stop_gradient(v)
            u_new = jax.lax.stop_gradient(u_new)
            sigma = u_new @ (W @ v)
            return W / sigma

        def _conv1x1(x, W, b, u):
            return jnp.einsum('bhwc,cd->bhwd', x, _sn(W, u)) + b
        key = jax.random.key(seed)
        ks = jax.random.split(key, 14)
        B, H, W, C = (8, 16, 16, 64)
        Cq = C // 8
        s = lambda fan_in: 1.0 / np.sqrt(fan_in)
        return {'x': jax.random.normal(ks[0], (B, H, W, C), jnp.float32), 'Wf': jax.random.normal(ks[1], (C, Cq), jnp.float32) * s(C), 'bf': jnp.zeros((Cq,), jnp.float32), 'uf': jax.random.normal(ks[2], (C,), jnp.float32), 'Wg': jax.random.normal(ks[3], (C, Cq), jnp.float32) * s(C), 'bg': jnp.zeros((Cq,), jnp.float32), 'ug': jax.random.normal(ks[4], (C,), jnp.float32), 'Wh': jax.random.normal(ks[5], (C, C), jnp.float32) * s(C), 'bh': jnp.zeros((C,), jnp.float32), 'uh': jax.random.normal(ks[6], (C,), jnp.float32), 'Wc': jax.random.normal(ks[7], (C, C), jnp.float32) * s(C), 'bc': jnp.zeros((C,), jnp.float32), 'uc': jax.random.normal(ks[8], (C,), jnp.float32), 'gamma': jnp.float32(0.7)}
    _L0_conv_all = _L0_conv_setup()
    _L0_conv_in = {k: v for k, v in _L0_conv_all.items() if k in ('Wf', 'bf', 'uf', 'Wg', 'bg', 'ug', 'Wh', 'bh', 'uh', 'Wc', 'bc', 'uc', 'gamma')}
    del _L0_conv_all
    return {'x': x, 'L0_conv_Wf': _L0_conv_in['Wf'], 'L0_conv_bf': _L0_conv_in['bf'], 'L0_conv_uf': _L0_conv_in['uf'], 'L0_conv_Wg': _L0_conv_in['Wg'], 'L0_conv_bg': _L0_conv_in['bg'], 'L0_conv_ug': _L0_conv_in['ug'], 'L0_conv_Wh': _L0_conv_in['Wh'], 'L0_conv_bh': _L0_conv_in['bh'], 'L0_conv_uh': _L0_conv_in['uh'], 'L0_conv_Wc': _L0_conv_in['Wc'], 'L0_conv_bc': _L0_conv_in['bc'], 'L0_conv_uc': _L0_conv_in['uc'], 'L0_conv_gamma': _L0_conv_in['gamma']}

def reference(x, L0_conv_Wf, L0_conv_bf, L0_conv_uf, L0_conv_Wg, L0_conv_bg, L0_conv_ug, L0_conv_Wh, L0_conv_bh, L0_conv_uh, L0_conv_Wc, L0_conv_bc, L0_conv_uc, L0_conv_gamma):
    import jax
    import jax.numpy as jnp

    def _L0_conv_ref(x, Wf, bf, uf, Wg, bg, ug, Wh, bh, uh, Wc, bc, uc, gamma):
        import jax, jax.numpy as jnp
        import numpy as np

        def _l2n(v, eps=1e-12):
            return v / (jnp.linalg.norm(v) + eps)

        def _sn(W, u):
            v = _l2n(W.T @ u)
            u_new = _l2n(W @ v)
            v = jax.lax.stop_gradient(v)
            u_new = jax.lax.stop_gradient(u_new)
            sigma = u_new @ (W @ v)
            return W / sigma

        def _conv1x1(x, W, b, u):
            return jnp.einsum('bhwc,cd->bhwd', x, _sn(W, u)) + b
        B, H, W, C = x.shape
        N = H * W
        flat = lambda t: t.reshape(B, N, t.shape[-1])
        f = flat(_conv1x1(x, Wf, bf, uf))
        g = flat(_conv1x1(x, Wg, bg, ug))
        h = flat(_conv1x1(x, Wh, bh, uh))
        s = jnp.einsum('bqd,bkd->bqk', g, f)
        beta = jax.nn.softmax(s, axis=-1)
        o = jnp.einsum('bqk,bkc->bqc', beta, h)
        o = o.reshape(B, H, W, C)
        o = _conv1x1(o, Wc, bc, uc)
        return gamma * o + x

    def _gn(v, G=32, eps=1e-05):
        B_, H_, W_, C_ = v.shape
        g = v.reshape(B_, H_, W_, G, C_ // G)
        m = jnp.mean(g, axis=(1, 2, 4), keepdims=True)
        s = jnp.var(g, axis=(1, 2, 4), keepdims=True)
        return ((g - m) / jnp.sqrt(s + eps)).reshape(v.shape)

    def _ln_c(v, eps=1e-06):
        m = jnp.mean(v, axis=-1, keepdims=True)
        s = jnp.var(v, axis=-1, keepdims=True)
        return (v - m) / jnp.sqrt(s + eps)

    def _ln_t(v, eps=1e-05):
        m = jnp.mean(v, axis=-1, keepdims=True)
        s = jnp.var(v, axis=-1, keepdims=True)
        return (v - m) / jnp.sqrt(s + eps)

    def _to_tokens(v):
        B_, H_, W_, C_ = v.shape
        return v.reshape(B_, H_ * W_, C_)

    def _from_tokens(t, like):
        return t.reshape(like.shape)
    x = _L0_conv_ref(x, L0_conv_Wf, L0_conv_bf, L0_conv_uf, L0_conv_Wg, L0_conv_bg, L0_conv_ug, L0_conv_Wh, L0_conv_bh, L0_conv_uh, L0_conv_Wc, L0_conv_bc, L0_conv_uc, L0_conv_gamma)
    return x

_drawn_inputs = setup_inputs


def setup_inputs(seed=0):
    import zlib

    import numpy as np

    out = dict(_drawn_inputs(seed))
    spreads = {'L0_conv_bf': (0.0, 0.8),
     'L0_conv_bg': (0.0, 0.369),
     'L0_conv_bh': (0.0, 0.1),
     'L0_conv_bc': (0.0, 0.1)}
    factors = {'L0_conv_uh': 3.383, 'L0_conv_uc': 3.322}
    for name, (base, spread) in spreads.items():
        noise = np.random.default_rng([zlib.crc32(name.encode()), seed]).standard_normal(out[name].shape)
        drawn = base * np.exp(spread * noise) if base else spread * noise
        out[name] = jnp.asarray(drawn.astype(out[name].dtype))
    for name, factor in factors.items():
        out[name] = (out[name] * factor).astype(out[name].dtype)
    return out
```

```python
from contextlib import ExitStack

import numpy as np

import concourse.bass as bass
from concourse import mybir

P = 128
B, N, C, D = 8, 256, 64, 8
CHUNKS = 2
SETS = B // CHUNKS
PAIRS = SETS // 2
J = N // P
ROWS = P // SETS
BLOCKS = ROWS // D
V1 = C + 1
EPS = 1e-12

F32 = mybir.dt.float32
F32R = mybir.dt.float32r
ALU = mybir.AluOpType
ACT = mybir.ActivationFunctionType
AX_X = mybir.AxisListType.X

COLS = {}
_at = 0
for _name, _n in (("w_fg", D), ("w_hc", C), ("u_fg", 1), ("u_hc", 1), ("norm_rhs", 8), ("half", 2), ("b_h", 1),
                  ("w_g", 2 * ROWS), ("w_f", 2 * ROWS), ("bias_g", 1), ("bias_f", 1), ("neg_level_g", 1),
                  ("neg_level_f", 1), ("gamma", 1), ("w_hT", P), ("b_c", C)):
    COLS[_name] = (_at, _at + _n)
    _at += _n
NCONST = _at
NORM_CONST = COLS["w_g"][0]


def attention(nc, xt, x, consts, out):
    x_tok = x.rearrange("(s c) (p j) f -> c p s (j f)", c=CHUNKS, j=J)
    out_tok = out.rearrange("(s c) (p j) f -> c p s (j f)", c=CHUNKS, j=J)

    with ExitStack() as ctx:
        def sb(name, shape, dt=F32):
            return ctx.enter_context(nc.sbuf_tensor(name, shape, dt))

        def bank(name):
            return ctx.enter_context(nc.psum_tensor(name, [P, 512], F32))

        def sem(name):
            return ctx.enter_context(nc.semaphore(name))

        cst = sb("cst", [P, NCONST])
        x_t = sb("x_t", [P, CHUNKS, PAIRS, N])
        x_sb = sb("x_sb", [P, CHUNKS, SETS, J, C])
        y = sb("y", [P, 2])
        junk = sb("junk", [P, D + C])
        twice_norm = sb("twice_norm", [P, 2, 4])
        root = sb("root", [P, 8])
        recip_root = sb("recip_root", [P, 8])
        newton = sb("newton", [P, 8])
        r_y = sb("r_y", [P, 2, 2])
        r_w = sb("r_w", [P, 2, 2])
        r_w1 = sb("r_w1", [P, 2, 2])
        inv_sigma = sb("inv_sigma", [P, 2, 2])
        inv_hc = sb("inv_hc", [P, 1])
        v_scale = sb("v_scale", [P, 1])
        bh_wc_row = sb("bh_wc_row", [P, C])
        bias_row = sb("bias_row", [P, C])
        bias_out = sb("bias_out", [P, C])
        w_v = sb("w_v", [P, 2, C])
        gf = sb("gf", [P, CHUNKS, 2, N])
        gf_hi = sb("gf_hi", [P, CHUNKS, 2, N], F32R)
        g_op = sb("g_op", [P, CHUNKS, N], F32R)
        f_lv = sb("f_lv", [P, CHUNKS, N], F32R)
        f_op = sb("f_op", [P, SETS, CHUNKS, N], F32R)
        ident = sb("ident", [P, P])
        neg_ones = sb("neg_ones", [P, P], F32R)
        v_sb = sb("v_sb", [P, CHUNKS, PAIRS, J, 2, V1])
        row_max = sb("row_max", [P, B, J])
        max_diag = sb("max_diag", [P, 2, J, P], F32R)
        p_t = sb("p_t", [P, 3, J, N])
        r_sum = sb("r_sum", [P, B, J])
        o_sb = sb("o_sb", [P, B, J, C])
        one = nc.const_aps.tensor(1.0, [P, 1], mybir.dt.bfloat16)
        table_out = sb("table_out", [P, 2])

        ps_norm = bank("ps_norm")
        ps_gf = [bank("ps_gf0"), bank("ps_gf1")]
        ps_s = [bank("ps_s0"), bank("ps_s1")]
        ps_st = [bank("ps_st0"), bank("ps_st1")]
        ps_v = bank("ps_v")

        def const(name, lo=0, hi=P):
            a, b = COLS[name]
            return cst[lo:hi, a:b]

        norm_consts_in = sem("norm_consts_in")
        consts_in = sem("consts_in")
        xt_in = [sem("xt_in0"), sem("xt_in1")]
        x_in = [sem("x_in0"), sem("x_in1")]
        zeros_set = sem("zeros_set")
        ident_zero = sem("ident_zero")
        ident_set = sem("ident_set")
        ones_set = sem("ones_set")
        t_ready = sem("t_ready")
        y_ready = sem("y_ready")
        norm_rhs_ready = sem("norm_rhs_ready")
        norms_ready = sem("norms_ready")
        roots_ready = sem("roots_ready")
        sigma_step = sem("sigma_step")
        sigma_ready = sem("sigma_ready")
        v_scale_ready = sem("v_scale_ready")
        bias_step = sem("bias_step")
        bias_ready = sem("bias_ready")
        x_bias_ready = sem("x_bias_ready")
        wv_ready = sem("wv_ready")
        bh_wc_ready = sem("bh_wc_ready")
        bh_wc_scaled = sem("bh_wc_scaled")
        wv_copied = sem("wv_copied")
        gf_ready = sem("gf_ready")
        g_copied = [sem(f"g_copied{c}") for c in range(CHUNKS)]
        f_copied = [sem(f"f_copied{c}") for c in range(CHUNKS)]
        g_hi_ready = [sem(f"g_hi_ready{c}") for c in range(CHUNKS)]
        f_hi_ready = [sem(f"f_hi_ready{c}") for c in range(CHUNKS)]
        g_ready = [sem(f"g_ready{c}") for c in range(CHUNKS)]
        f_level_ready = [sem(f"f_level_ready{c}") for c in range(CHUNKS)]
        f_ready = [[sem(f"f_ready{c}{s}") for s in range(SETS)] for c in range(CHUNKS)]
        v_ready = sem("v_ready")
        v_copied = sem("v_copied")
        scores_ready = sem("scores_ready")
        max_ready = sem("max_ready")
        diag_ready = sem("diag_ready")
        scores_t_ready = sem("scores_t_ready")
        probs_ready = sem("probs_ready")
        out_ready = sem("out_ready")
        recip_ready = sem("recip_ready")
        scaled = sem("scaled")
        summed = sem("summed")
        last_done = sem("last_done")
        stored = sem("stored")

        block = ctx.enter_context(nc.Block())

        def values(ps):
            return ps[:, :].rearrange("p (a j e f) -> p a j e f", a=PAIRS, j=J, e=2)

        norm_rhs = const("norm_rhs").rearrange("p (n a) -> p n a", n=2)
        squares = ps_norm[:, 256:264]

        bh_wc = ps_st[1][:, 0:C]

        def outputs(k):
            return ps_gf[k % 2][:, 0:2 * J * V1].rearrange("p (b j f) -> p b j f", b=2, j=J)

        def output(i, j):
            if i == B - 1:
                return [ps_norm, ps_v][j][:, 0:V1]
            return outputs(i // 2)[:, i % 2, j]

        @block.sync
        def _(sp):
            sp.dma_start(cst[:, 0:NORM_CONST], consts[:, 0:NORM_CONST]).then_inc(norm_consts_in, 16)
            sp.dma_start(cst[:, NORM_CONST:], consts[:, NORM_CONST:]).then_inc(consts_in, 16)
            sp.dma_start(x_t[:, 1], xt[:, 1]).then_inc(xt_in[1], 16)
            for c in range(CHUNKS):
                sp.dma_start(x_sb[:, c].rearrange("p s j f -> p s (j f)"), x_tok[c]).then_inc(x_in[c], 16)
            for k in range(B // 2 - 1):
                c, s = divmod(2 * k, SETS)
                sp.wait_ge(summed, k + 1)
                sp.dma_start(out_tok[c][:, s:s + 2],
                             o_sb[:, 2 * k:2 * k + 2].rearrange("p b j f -> p b (j f)")).then_inc(stored, 16)
            for i in (B - 2, B - 1):
                sp.wait_ge(last_done, J * (i - (B - 2)) + J)
                sp.dma_start(out_tok[i // SETS][:, i % SETS],
                             o_sb[:, i].rearrange("p j f -> p (j f)")).then_inc(stored, 16)
            sp.wait_ge(stored, 16 * (B // 2 + 1))

        @block.gpsimd
        def _(pool):
            pool.memset(ident[:, :], 0.0).then_inc(ident_zero, 1)
            pool.wait_ge(ident_zero, 1)
            pool.affine_select(out=ident[:, :], in_=ident[:, :], compare_op=ALU.not_equal, fill=1.0, base=0,
                               pattern=[[-1, P]], channel_multiplier=1).then_inc(ident_set, 1)
            pool.memset(v_sb[:, :, :, :, :, C:V1], 1.0).then_inc(ones_set, 1)
            pool.wait_ge(consts_in, 16)
            pool.wait_ge(sigma_ready, 1)
            pool.tensor_tensor(inv_hc[:, :], inv_sigma[:, 1, 0:1], inv_sigma[:, 1, 1:2], ALU.mult).then_inc(bias_step, 1)
            pool.wait_ge(bias_step, 1)
            pool.tensor_tensor(v_scale[:, :], inv_hc[:, :], const("gamma"), ALU.mult).then_inc(v_scale_ready, 1)
            pool.wait_ge(bh_wc_scaled, 1)
            pool.tensor_tensor(bias_row[:, :], bh_wc_row[:, :], const("b_c"), ALU.add).then_inc(bias_step, 1)
            pool.wait_ge(bias_step, 2)
            pool.tensor_scalar(bias_out[:, :], bias_row[:, :], const("gamma"), None, ALU.mult).then_inc(bias_ready, 1)

            pool.wait_ge(bias_ready, 1)
            for c in range(CHUNKS):
                pool.wait_ge(x_in[c], 16)
                xs = x_sb[:, c].rearrange("p s j f -> p (s j) f")
                pool.tensor_tensor(xs, xs, bias_out[:, :].unsqueeze(1).to_broadcast([P, SETS * J, C]),
                                   ALU.add).then_inc(x_bias_ready, 1)

            for k in range(B // 2 - 1):
                c, s = divmod(2 * k, SETS)
                pool.wait_ge(scaled, k + 1)
                pool.wait_ge(x_bias_ready, c + 1)
                pool.tensor_tensor(o_sb[:, 2 * k:2 * k + 2], o_sb[:, 2 * k:2 * k + 2], x_sb[:, c, s:s + 2],
                                   ALU.add).then_inc(summed, 1)

        @block.scalar
        def _(act):
            act.dma_start(x_t[:, 0], xt[:, 0]).then_inc(xt_in[0], 16)
            act.activation(table_out[:, 0:1], one, ACT.Sqrt)
            act.wait_ge(norms_ready, 1)
            act.activation(root[:, :], squares, ACT.Sqrt).then_inc(roots_ready, 1)
            act.activation(table_out[:, 1:2], one, ACT.Exp)
            act.wait_ge(wv_ready, 1)
            act.wait_ge(zeros_set, 1)
            for e in range(2):
                act.activation(w_v[C * e:C * e + C, e, :], ps_v[C * e:C * e + C, 0:C], ACT.Copy).then_inc(wv_copied, 1)
            act.wait_ge(sigma_ready, 1)

            def project(c, name, n, w):
                act.wait_ge(gf_ready, c + 1)
                act.activation(gf[:, c, n], ps_gf[c][:, N * n:N * n + N], ACT.Identity, bias=const(name),
                               scale=inv_sigma[:, 0, w:w + 1]).then_inc([g_copied, f_copied][n][c], 1)

            def first_part(c, n):
                act.wait_ge([g_copied, f_copied][n][c], 1)
                act.activation(gf_hi[:, c, n], gf[:, c, n], ACT.Copy).then_inc([g_hi_ready, f_hi_ready][n][c], 1)

            def place_f(c, s):
                rows = slice(ROWS * s, ROWS * s + ROWS)
                act.wait_ge(f_level_ready[c], 1)
                act.wait_ge(zeros_set, 3)
                act.activation(f_op[rows, s, c], f_lv[rows, c], ACT.Copy).then_inc(f_ready[c][s], 1)

            def copy_values(c):
                act.wait_ge(v_ready, c + 1)
                act.wait_ge(v_scale_ready, 1)
                act.activation(v_sb[:, c, :, :, :, 0:C], values([ps_v, ps_norm][c]), ACT.Copy,
                               scale=v_scale[:, 0:1]).then_inc(v_copied, 1)

            project(0, "bias_g", 0, 1)
            act.wait_ge(bh_wc_ready, 1)
            act.activation(bh_wc_row[:, :], bh_wc, ACT.Copy, scale=inv_sigma[:, 1, 1:2]).then_inc(bh_wc_scaled, 1)
            first_part(0, 0)
            project(1, "bias_f", 1, 0)
            place_f(0, 1)
            first_part(1, 1)
            place_f(0, 2)
            project(1, "bias_g", 0, 1)
            first_part(1, 0)
            place_f(0, 3)
            copy_values(0)
            for i in range(B):
                act.wait_ge(scores_t_ready, i + 1)
                if i >= 3:
                    act.wait_ge(out_ready, J * (i - 2))
                act.activation(p_t[:, i % 3].rearrange("p j n -> p (j n)"), ps_st[i % 2][:, :],
                               ACT.Exp).then_inc(probs_ready, 1)
                if i == 0:
                    place_f(1, 0)
                if i == 1:
                    place_f(1, 1)
                    copy_values(1)
                if i == 2:
                    place_f(1, 2)
                if i == 3:
                    place_f(1, 3)

        @block.vector
        def _(dve):
            dve.memset(w_v[:, :, :], 0.0).then_inc(zeros_set, 1)
            dve.memset(neg_ones[:, :].bitcast(F32), -1.0).then_inc(zeros_set, 1)
            dve.memset(f_op[:, :, :, :].bitcast(F32), 0.0).then_inc(zeros_set, 1)

            dve.wait_ge(t_ready, 1)
            dve.wait_ge(norm_consts_in, 16)
            for n, (name, lo, w) in enumerate((("w_fg", 0, D), ("w_hc", D, C))):
                dve.tensor_tensor_reduce(junk[:, lo:lo + w], ps_norm[:, lo:lo + w], const(name), 1.0, 0.0, ALU.mult,
                                         ALU.add, y[:, n:n + 1]).then_inc(y_ready, 1)
            dve.wait_ge(y_ready, 2)
            dve.tensor_tensor(norm_rhs[:, :, 0:2], const("half").unsqueeze(1).to_broadcast([P, 2, 2]),
                              y[:, :].unsqueeze(2).to_broadcast([P, 2, 2]), ALU.mult).then_inc(norm_rhs_ready, 1)
            dve.wait_ge(roots_ready, 1)
            dve.reciprocal(recip_root[:, :], root[:, :]).then_inc(sigma_step, 1)
            dve.wait_ge(sigma_step, 1)
            dve.tensor_tensor(newton[:, :], squares, recip_root[:, :], ALU.mult).then_inc(sigma_step, 1)
            dve.wait_ge(sigma_step, 2)
            dve.tensor_tensor(twice_norm[:, :, :].rearrange("p n a -> p (n a)"), newton[:, :], root[:, :],
                              ALU.add).then_inc(sigma_step, 1)
            dve.wait_ge(sigma_step, 3)
            dve.reciprocal(r_y[:, :, :], twice_norm[:, :, 0:2]).then_inc(sigma_step, 1)
            dve.wait_ge(sigma_step, 4)
            dve.scalar_tensor_tensor(out=r_w[:, :, :], in0=twice_norm[:, :, 2:4], scalar=2 * EPS, in1=r_y[:, :, :],
                                     op0=ALU.add, op1=ALU.mult).then_inc(sigma_step, 1)
            dve.wait_ge(sigma_step, 5)
            dve.tensor_scalar(r_w1[:, :, :], r_w[:, :, :], EPS, 1.0, ALU.mult, ALU.add).then_inc(sigma_step, 1)
            dve.wait_ge(sigma_step, 6)
            dve.tensor_tensor(inv_sigma[:, :, :], r_w1[:, :, :], r_w[:, :, :], ALU.mult).then_inc(sigma_ready, 1)
            dve.wait_ge(sigma_ready, 1)
            def split_f(c):
                dve.wait_ge(f_hi_ready[c], 1)
                dve.scalar_tensor_tensor(out=f_lv[:, c], in0=gf_hi[:, c, 1].bitcast(F32), scalar=const("neg_level_f"),
                                         in1=gf[:, c, 1], op0=ALU.mult, op1=ALU.add).then_inc(f_level_ready[c], 1)

            def split_g(c):
                dve.wait_ge(g_hi_ready[c], 1)
                dve.scalar_tensor_tensor(out=g_op[:, c], in0=gf_hi[:, c, 0].bitcast(F32), scalar=const("neg_level_g"),
                                         in1=gf[:, c, 0], op0=ALU.mult, op1=ALU.add).then_inc(g_ready[c], 1)

            dve.wait_ge(gf_ready, 1)
            dve.wait_ge(consts_in, 16)
            dve.tensor_scalar(gf[:, 0, 1], ps_st[0][:, 0:N], inv_sigma[:, 0, 0:1], const("bias_f"), ALU.mult,
                              ALU.add).then_inc(f_copied[0], 1)
            dve.wait_ge(f_copied[0], 1)
            dve.tensor_copy(gf_hi[:, 0, 1], gf[:, 0, 1]).then_inc(f_hi_ready[0], 1)
            split_f(0)
            split_g(0)
            dve.wait_ge(f_level_ready[0], 1)
            dve.tensor_copy(f_op[0:ROWS, 0, 0], f_lv[0:ROWS, 0]).then_inc(f_ready[0][0], 1)

            def maxima(i):
                dve.wait_ge(scores_ready, i + 1)
                dve.tensor_reduce(row_max[:, i], ps_s[i % 2][:, :].rearrange("p (j n) -> p j n", j=J), AX_X,
                                  ALU.max).then_inc(max_ready, 1)

            def diagonal(i):
                dve.wait_ge(max_ready, i + 1)
                if i >= 2:
                    dve.wait_ge(scores_t_ready, i - 1)
                dve.tensor_tensor(max_diag[:, i % 2], ident[:, :].unsqueeze(1).to_broadcast([P, J, P]),
                                  row_max[:, i].unsqueeze(2).to_broadcast([P, J, P]), ALU.mult).then_inc(diag_ready, 1)

            def finish(k):
                dve.wait_ge(out_ready, J * (2 * k + 2))
                dve.reciprocal(r_sum[:, 2 * k:2 * k + 2], outputs(k)[:, :, :, C]).then_inc(recip_ready, 1)
                dve.wait_ge(recip_ready, k + 1)
                dve.tensor_tensor(o_sb[:, 2 * k:2 * k + 2], outputs(k)[:, :, :, 0:C],
                                  r_sum[:, 2 * k:2 * k + 2].unsqueeze(3).to_broadcast([P, 2, J, C]),
                                  ALU.mult).then_inc(scaled, 1)

            dve.wait_ge(ident_set, 1)
            maxima(0)
            for i in range(B):
                diagonal(i)
                if i == 0:
                    split_f(1)
                if i == 1:
                    split_g(1)
                if i + 1 < B:
                    maxima(i + 1)
                if i % 2 == 1 and i >= 3:
                    finish(i // 2 - 1)
            dve.wait_ge(x_bias_ready, CHUNKS)
            for i in (B - 2, B - 1):
                for j in range(J):
                    dve.wait_ge(out_ready, J * i + (J if i < B - 1 else j + 1))
                    dve.reciprocal(r_sum[:, i, j:j + 1], output(i, j)[:, C:V1]).then_inc(recip_ready, 1)
                    dve.wait_ge(recip_ready, B // 2 - 1 + J * (i - (B - 2)) + j + 1)
                    dve.scalar_tensor_tensor(out=o_sb[:, i, j], in0=output(i, j)[:, 0:C],
                                             scalar=r_sum[:, i, j:j + 1], in1=x_sb[:, i // SETS, i % SETS, j],
                                             op0=ALU.mult, op1=ALU.add).then_inc(last_done, 1)

        @block.tensor
        def _(pe):
            mm = nc.tensor.matmul
            for _ in range(WARM):
                mm(ps_s[0][:, 0:256], one.to_broadcast([P, P]), one.to_broadcast([P, 256]),
                   start=True, stop=True)

            pe.wait_ge(norm_consts_in, 16)
            for lo in (0, C):
                rows = (lo, lo + C)
                for u, w, col, n in (("u_fg", "w_fg", 0, D), ("u_hc", "w_hc", D, C)):
                    last = mm(ps_norm[lo:lo + C, col:col + n], const(u, *rows).to_broadcast([C, C]), const(w, *rows),
                              start=True, stop=True)
            last.then_inc(t_ready, 1)

            def project(c):
                pe.wait_ge(xt_in[c], 16)
                for n, w in enumerate(("w_g", "w_f")):
                    for a in range(PAIRS):
                        ps = ps_st[0][:, 0:N] if (c, n) == (0, 1) else ps_gf[c][:, N * n:N * n + N]
                        last = mm(ps[2 * ROWS * a:2 * ROWS * (a + 1)], const(w), x_t[:, c, a],
                                  start=True, stop=True)
                last.then_inc(gf_ready, 1)

            def values_of(c):
                if c == 0:
                    pe.wait_ge(wv_copied, 2)
                else:
                    pe.wait_ge(sigma_step, 2)
                ps = values([ps_v, ps_norm][c])
                for a in range(PAIRS):
                    for j in range(J):
                        last = mm(ps[:, a, j].rearrange("p e f -> p (e f)"), x_t[:, c, a, P * j:P * j + P],
                                  w_v[:, :, :].rearrange("p e f -> p (e f)"), start=True, stop=True)
                last.then_inc(v_ready, 1)

            def scores(i):
                c, s = divmod(i, SETS)
                pe.wait_ge(g_ready[c], 1)
                pe.wait_ge(f_ready[c][s], 1)
                if i >= 2:
                    pe.wait_ge(max_ready, i - 1)
                for j in range(J):
                    last = mm(ps_s[i % 2][:, N * j:N * j + N], g_op[:, c, P * j:P * j + P], f_op[:, s, c],
                              start=True, stop=True)
                last.then_inc(scores_ready, 1)

            def scores_t_bank(i):
                return ps_st[i % 2][:, :].rearrange("p (k n) -> p k n", k=J)

            def scores_t(i):
                c, s = divmod(i, SETS)
                if i >= 2:
                    pe.wait_ge(probs_ready, i - 1)
                ps = scores_t_bank(i)
                for k in range(J):
                    mm(ps[:, k], f_op[:, s, c, P * k:P * k + P], g_op[:, c], start=(k == 0), stop=False,
                       skip_group_check=True)

            def subtract_maxima(i):
                pe.wait_ge(diag_ready, i + 1)
                for j in range(J):
                    last = mm(scores_t_bank(i)[:, :, P * j:P * j + P], neg_ones[:, :],
                              max_diag[:, i % 2, j].unsqueeze(1).to_broadcast([P, J, P]), start=False,
                              stop=(j == J - 1), skip_group_check=True)
                last.then_inc(scores_t_ready, 1)

            def attend(i):
                c, s = divmod(i, SETS)
                a, e = divmod(s, 2)
                pe.wait_ge(probs_ready, i + 1)
                pe.wait_ge(v_copied, c + 1)
                if i % 2 == 0:
                    if i >= 4:
                        pe.wait_ge(scaled, i // 2 - 1)
                    else:
                        pe.wait_ge(g_copied[i // 2], 1)
                        pe.wait_ge(f_copied[i // 2], 1)
                if i == 0:
                    pe.wait_ge(ones_set, 1)
                for j in range(J):
                    for k in range(J):
                        last = mm(output(i, j), p_t[:, i % 3, k, P * j:P * j + P],
                                  v_sb[:, c, a, k, e], start=(k == 0), stop=(k == J - 1))
                    last.then_inc(out_ready, 1)

            pe.wait_ge(norm_rhs_ready, 1)
            for n in range(2):
                last = mm(squares[:, 4 * n:4 * n + 4], y[:, n:n + 1].to_broadcast([P, P]), norm_rhs[:, n],
                          start=True, stop=True)
            last.then_inc(norms_ready, 1)
            pe.wait_ge(consts_in, 16)
            project(0)
            mm(ps_v[:, 0:C], const("w_hT", C, P), const("w_hc", C, P), start=True, stop=True).then_inc(wv_ready, 1)
            mm(bh_wc, const("b_h", C, P).to_broadcast([C, P]), const("w_hc", C, P), start=True,
               stop=True).then_inc(bh_wc_ready, 1)
            project(1)
            values_of(0)
            pe.wait_ge(zeros_set, 3)
            scores(0)
            scores(1)
            for i in range(B):
                if i == 1:
                    pe.wait_ge(bh_wc_scaled, 1)
                scores_t(i)
                if i == 0:
                    values_of(1)
                if i + 2 < B:
                    scores(i + 2)
                if i >= 2:
                    attend(i - 2)
                subtract_maxima(i)
            attend(B - 2)
            attend(B - 1)


WARM = 15


def pack_constants(Wf, bf, uf, Wg, bg, ug, Wh, bh, uh, Wc, bc, uc, gamma):
    z = np.zeros((P, NCONST), np.float32)

    def col(name):
        return z[:, COLS[name][0]:COLS[name][1]]

    col("w_fg")[:C], col("w_fg")[C:] = Wf, Wg
    col("w_hc")[:C], col("w_hc")[C:] = Wh, Wc
    col("u_fg")[:, 0] = np.concatenate([uf, ug])
    col("u_hc")[:, 0] = np.concatenate([uh, uc])
    for n, u in enumerate((uf, ug, uh, uc)):
        col("norm_rhs")[C * (n % 2):C * (n % 2) + C, 4 * (n // 2) + 2 + n % 2] = u
    col("half")[:C, 0] = 1.0
    col("half")[C:, 1] = 1.0
    col("bias_g")[:, 0] = np.tile(bg, P // D)
    col("bias_f")[:, 0] = np.tile(bf, P // D)
    part = np.arange(P) // D % BLOCKS
    col("neg_level_g")[:, 0] = np.where(part // 2 == 1, -1.0, 0.0)
    col("neg_level_f")[:, 0] = np.where(part % 2 == 1, -1.0, 0.0)
    col("gamma")[:] = gamma
    col("b_h")[C:, 0] = bh
    for e in range(2):
        rows, cols = slice(C * e, C * e + C), slice(ROWS * e, ROWS * e + ROWS)
        col("w_g")[rows, cols] = np.tile(Wg, (1, BLOCKS))
        col("w_f")[rows, cols] = np.tile(Wf, (1, BLOCKS))
        col("w_hT")[C:, C * e:C * e + C] = Wh.T
    col("b_c")[:] = bc
    return z


def kernel(**inputs):
    import numpy as _np
    import concourse.bacc as _bacc
    from concourse.bass_utils import run_bass_kernel_spmd as _run

    a = {k.replace("L0_conv_", ""): _np.asarray(v) for k, v in inputs.items()}
    x = a.pop("x")
    shape = x.shape
    xt = x.reshape(PAIRS, 2, CHUNKS, P, J, C).transpose(1, 5, 2, 0, 4, 3).reshape(P, CHUNKS, PAIRS, N)
    arrays = {"in_xt": _np.ascontiguousarray(xt), "in_x": _np.ascontiguousarray(x.reshape(B, N, C)),
              "in_consts": pack_constants(**a)}
    nc = _bacc.Bacc("TRN2", target_bir_lowering=False, num_devices=1)
    args = [nc.dram_tensor(k, v.shape, F32, kind="ExternalInput").ap() for k, v in arrays.items()]
    out = nc.dram_tensor("out", (B, N, C), F32, kind="ExternalOutput").ap()
    attention(nc, *args, out)
    r = _run(nc, [arrays], core_ids=[0])
    return r.results[0]["out"].reshape(shape)
```

```python
from contextlib import ExitStack

import numpy as np

import concourse.bass as bass
from concourse import mybir

P = 128
B, N, C, D = 8, 256, 64, 8
CHUNKS = 2
SETS = B // CHUNKS
PAIRS = SETS // 2
J = N // P
ROWS = P // SETS
BLOCKS = ROWS // D
V1 = C + 1
EPS = 1e-12
WARM_PRODUCTS = 15
BY_POOL = 5

F32 = mybir.dt.float32
F32R = mybir.dt.float32r
ALU = mybir.AluOpType
ACT = mybir.ActivationFunctionType
AX_X = mybir.AxisListType.X

COLS = {}
_at = 0
for _name, _n in (("w_fg", D), ("w_hc", C), ("u_fg", 1), ("u_hc", 1), ("norm_rhs", 8), ("half", 2), ("b_h", 1),
                  ("w_g", 2 * ROWS), ("w_f", 2 * ROWS), ("bias_g", 1), ("bias_f", 1), ("neg_second_g", 1),
                  ("neg_second_f", 1), ("gamma", 1), ("w_hT", P), ("b_c", C)):
    COLS[_name] = (_at, _at + _n)
    _at += _n
NCONST = _at
NORM_CONST = COLS["w_g"][0]


def attention(nc, xt, x, consts, out):
    x_tok = x.rearrange("(s c) (p j) f -> c p s (j f)", c=CHUNKS, j=J)
    out_tok = out.rearrange("(s c) (p j) f -> c p s (j f)", c=CHUNKS, j=J)

    with ExitStack() as ctx:
        def sb(name, shape, dt=F32):
            return ctx.enter_context(nc.sbuf_tensor(name, shape, dt))

        def bank(name):
            return ctx.enter_context(nc.psum_tensor(name, [P, 512], F32))

        def sem(name):
            return ctx.enter_context(nc.semaphore(name))

        cst = sb("cst", [P, NCONST])
        x_t = sb("x_t", [P, CHUNKS, PAIRS, N])
        x_sb = sb("x_sb", [P, CHUNKS, SETS, J, C])
        y = sb("y", [P, 2])
        products = sb("products", [P, D + C])
        twice_norm = sb("twice_norm", [P, 2, 4])
        root = sb("root", [P, 8])
        recip_root = sb("recip_root", [P, 8])
        newton = sb("newton", [P, 8])
        r_y = sb("r_y", [P, 2, 2])
        r_w = sb("r_w", [P, 2, 2])
        r_w1 = sb("r_w1", [P, 2, 2])
        inv_sigma = sb("inv_sigma", [P, 2, 2])
        inv_hc = sb("inv_hc", [P, 1])
        v_scale = sb("v_scale", [P, 1])
        bh_wc_row = sb("bh_wc_row", [P, C])
        bias_row = sb("bias_row", [P, C])
        bias_out = sb("bias_out", [P, C])
        w_v = sb("w_v", [P, 2, C])
        gf = sb("gf", [P, CHUNKS, 2, N])
        gf_hi = sb("gf_hi", [P, CHUNKS, 2, N], F32R)
        neg_hi = sb("neg_hi", [P, N])
        g_parts = sb("g_parts", [P, CHUNKS, N], F32R)
        f_parts = sb("f_parts", [P, CHUNKS, N], F32R)
        ident = sb("ident", [P, P])
        neg_ones = sb("neg_ones", [P, P], F32R)
        v_sb = sb("v_sb", [P, CHUNKS, PAIRS, J, 2, V1])
        row_max = sb("row_max", [P, B, J])
        max_diag = sb("max_diag", [P, 2, J, P], F32R)
        p_t = sb("p_t", [P, 3, J, N])
        r_sum = sb("r_sum", [P, B, J])
        o_sb = sb("o_sb", [P, B, J, C])
        one = nc.const_aps.tensor(1.0, [P, 1], mybir.dt.bfloat16)
        table_out = sb("table_out", [P, 2])

        ps_norm = bank("ps_norm")
        ps_gf = [bank("ps_gf0"), bank("ps_gf1")]
        ps_s = [bank("ps_s0"), bank("ps_s1")]
        ps_st = [bank("ps_st0"), bank("ps_st1")]
        ps_v = bank("ps_v")

        OUT_BANKS = (ps_gf[0], ps_gf[1], ps_v)

        def const(name, lo=0, hi=P):
            a, b = COLS[name]
            return cst[lo:hi, a:b]

        norm_consts_in = sem("norm_consts_in")
        consts_in = sem("consts_in")
        xt_in = [sem("xt_in0"), sem("xt_in1")]
        x_in = [sem("x_in0"), sem("x_in1")]
        zeros_set = sem("zeros_set")
        ident_zero = sem("ident_zero")
        ident_set = sem("ident_set")
        ones_set = sem("ones_set")
        t_ready = sem("t_ready")
        y_ready = sem("y_ready")
        norm_rhs_ready = sem("norm_rhs_ready")
        norms_ready = sem("norms_ready")
        roots_ready = sem("roots_ready")
        sigma_step = sem("sigma_step")
        sigma_ready = sem("sigma_ready")
        v_scale_ready = sem("v_scale_ready")
        bias_step = sem("bias_step")
        bias_ready = sem("bias_ready")
        x_bias_ready = sem("x_bias_ready")
        wv_ready = sem("wv_ready")
        bh_wc_ready = sem("bh_wc_ready")
        bh_wc_scaled = sem("bh_wc_scaled")
        wv_copied = sem("wv_copied")
        gf_ready = sem("gf_ready")
        g_copied = [sem(f"g_copied{c}") for c in range(CHUNKS)]
        f_copied = [sem(f"f_copied{c}") for c in range(CHUNKS)]
        g_hi_ready = [sem(f"g_hi_ready{c}") for c in range(CHUNKS)]
        neg_hi_ready = sem("neg_hi_ready")
        f_hi_ready = [sem(f"f_hi_ready{c}") for c in range(CHUNKS)]
        g_ready = [sem(f"g_ready{c}") for c in range(CHUNKS)]
        f_ready = [sem(f"f_ready{c}") for c in range(CHUNKS)]
        v_ready = sem("v_ready")
        v_copied = sem("v_copied")
        scores_ready = sem("scores_ready")
        max_ready = sem("max_ready")
        diag_ready = sem("diag_ready")
        scores_t_ready = sem("scores_t_ready")
        probs_ready = sem("probs_ready")
        out_ready = sem("out_ready")
        recip_ready = sem("recip_ready")
        scaled = sem("scaled")
        summed = sem("summed")
        summed_last = sem("summed_last")
        stored = sem("stored")

        block = ctx.enter_context(nc.Block())

        def set_rows(s):
            return slice(ROWS * s, ROWS * s + ROWS)

        def values(ps):
            return ps[:, :].rearrange("p (a j e f) -> p a j e f", a=PAIRS, j=J, e=2)

        norm_rhs = const("norm_rhs").rearrange("p (n a) -> p n a", n=2)
        squares = ps_norm[:, 256:264]

        bh_wc = ps_st[1][:, 0:C]

        def scores_t_bank(i):
            return ps_st[i % 2][:, :].rearrange("p (k n) -> p k n", k=J)

        def output(i, j):
            return OUT_BANKS[i % len(OUT_BANKS)][:, V1 * j:V1 * j + V1]

        def out_sums(i):
            return OUT_BANKS[i % len(OUT_BANKS)][:, 0:J * V1].rearrange("p (j f) -> p j f", j=J)[:, :, C]

        @block.sync
        def _(sp):
            sp.dma_start(cst[:, 0:NORM_CONST], consts[:, 0:NORM_CONST]).then_inc(norm_consts_in, 16)
            sp.dma_start(cst[:, NORM_CONST:], consts[:, NORM_CONST:]).then_inc(consts_in, 16)
            sp.dma_start(x_t[:, 1], xt[:, 1]).then_inc(xt_in[1], 16)
            for c in range(CHUNKS):
                sp.dma_start(x_sb[:, c].rearrange("p s j f -> p s (j f)"), x_tok[c]).then_inc(x_in[c], 16)
            for k in range(B // 2):
                c, s = divmod(2 * k, SETS)
                sp.wait_ge(summed, min(2 * k + 2, BY_POOL))
                if 2 * k + 2 > BY_POOL:
                    sp.wait_ge(summed_last, J * (2 * k + 2 - BY_POOL))
                sp.dma_start(out_tok[c][:, s:s + 2],
                             o_sb[:, 2 * k:2 * k + 2].rearrange("p b j f -> p b (j f)")).then_inc(stored, 16)
            sp.wait_ge(stored, 16 * (B // 2))

        @block.gpsimd
        def _(pool):
            pool.memset(ident[:, :], 0.0).then_inc(ident_zero, 1)
            pool.wait_ge(ident_zero, 1)
            pool.affine_select(out=ident[:, :], in_=ident[:, :], compare_op=ALU.not_equal, fill=1.0, base=0,
                               pattern=[[-1, P]], channel_multiplier=1).then_inc(ident_set, 1)
            pool.memset(v_sb[:, :, :, :, :, C:V1], 1.0).then_inc(ones_set, 1)
            pool.wait_ge(consts_in, 16)
            pool.wait_ge(sigma_ready, 1)
            pool.tensor_tensor(inv_hc[:, :], inv_sigma[:, 1, 0:1], inv_sigma[:, 1, 1:2],
                               ALU.mult).then_inc(bias_step, 1)
            pool.wait_ge(bias_step, 1)
            pool.tensor_tensor(v_scale[:, :], inv_hc[:, :], const("gamma"), ALU.mult).then_inc(v_scale_ready, 1)
            pool.wait_ge(bh_wc_scaled, 1)
            pool.tensor_tensor(bias_row[:, :], bh_wc_row[:, :], const("b_c"), ALU.add).then_inc(bias_step, 1)
            pool.wait_ge(bias_step, 2)
            pool.tensor_scalar(bias_out[:, :], bias_row[:, :], const("gamma"), None, ALU.mult).then_inc(bias_ready, 1)

            pool.wait_ge(bias_ready, 1)
            for c in range(CHUNKS):
                if c == 1:
                    pool.wait_ge(neg_hi_ready, 1)
                    pool.tensor_tensor(g_parts[:, 1], gf[:, 1, 0], neg_hi[:, :], ALU.add).then_inc(g_ready[1], 1)
                pool.wait_ge(x_in[c], 16)
                xs = x_sb[:, c].rearrange("p s j f -> p (s j) f")
                pool.tensor_tensor(xs, xs, bias_out[:, :].unsqueeze(1).to_broadcast([P, SETS * J, C]),
                                   ALU.add).then_inc(x_bias_ready, 1)

            for i in range(BY_POOL):
                c, s = divmod(i, SETS)
                pool.wait_ge(scaled, i + 1)
                pool.wait_ge(x_bias_ready, c + 1)
                pool.tensor_tensor(o_sb[:, i], o_sb[:, i], x_sb[:, c, s], ALU.add).then_inc(summed, 1)

        @block.scalar
        def _(act):
            act.dma_start(x_t[:, 0], xt[:, 0]).then_inc(xt_in[0], 16)
            act.activation(table_out[:, 0:1], one, ACT.Sqrt)
            act.wait_ge(norms_ready, 1)
            act.activation(root[:, :], squares, ACT.Sqrt).then_inc(roots_ready, 1)
            act.activation(table_out[:, 1:2], one, ACT.Exp)
            act.wait_ge(wv_ready, 1)
            act.wait_ge(zeros_set, 1)
            for e in range(2):
                act.activation(w_v[C * e:C * e + C, e, :], ps_v[C * e:C * e + C, 0:C], ACT.Copy).then_inc(wv_copied, 1)
            act.wait_ge(sigma_ready, 1)

            def project(c, name, n, w):
                act.wait_ge(gf_ready, c + 1)
                act.activation(gf[:, c, n], ps_gf[c][:, N * n:N * n + N], ACT.Identity, bias=const(name),
                               scale=inv_sigma[:, 0, w:w + 1]).then_inc([g_copied, f_copied][n][c], 1)

            def first_part(c, n):
                act.wait_ge([g_copied, f_copied][n][c], 1)
                act.activation(gf_hi[:, c, n], gf[:, c, n], ACT.Copy).then_inc([g_hi_ready, f_hi_ready][n][c], 1)

            def copy_values(c):
                act.wait_ge(v_ready, c + 1)
                act.wait_ge(v_scale_ready, 1)
                act.activation(v_sb[:, c, :, :, :, 0:C], values([ps_v, ps_norm][c]), ACT.Copy,
                               scale=v_scale[:, 0:1]).then_inc(v_copied, 1)

            def scale(i):
                act.wait_ge(recip_ready, i + 1)
                for j in range(J):
                    last = act.activation(o_sb[:, i, j], output(i, j)[:, 0:C], ACT.Copy, scale=r_sum[:, i, j:j + 1])
                last.then_inc(scaled, 1)

            project(0, "bias_g", 0, 1)
            act.wait_ge(bh_wc_ready, 1)
            act.activation(bh_wc_row[:, :], bh_wc, ACT.Copy, scale=inv_sigma[:, 1, 1:2]).then_inc(bh_wc_scaled, 1)
            first_part(0, 0)
            project(1, "bias_f", 1, 0)
            first_part(1, 1)
            project(1, "bias_g", 0, 1)
            first_part(1, 0)
            act.wait_ge(g_hi_ready[1], 1)
            act.activation(neg_hi[:, :], gf_hi[:, 1, 0].bitcast(F32), ACT.Copy,
                           scale=const("neg_second_g")).then_inc(neg_hi_ready, 1)
            copy_values(0)
            for i in range(B):
                act.wait_ge(scores_t_ready, i + 1)
                if i >= 3:
                    act.wait_ge(out_ready, J * (i - 2))
                if i < B - 1:
                    act.activation(p_t[:, i % 3].rearrange("p k n -> p (k n)"), ps_st[i % 2][:, :],
                                   ACT.Exp).then_inc(probs_ready, 1)
                else:
                    for j in range(J):
                        tile = slice(P * j, P * j + P)
                        act.activation(p_t[:, i % 3, :, tile], scores_t_bank(i)[:, :, tile],
                                       ACT.Exp).then_inc(probs_ready, 1)
                if i == 1:
                    copy_values(1)
                if 2 <= i < BY_POOL + 2:
                    scale(i - 2)

        @block.vector
        def _(dve):
            dve.memset(w_v[:, :, :], 0.0).then_inc(zeros_set, 1)
            dve.memset(neg_ones[:, :].bitcast(F32), -1.0).then_inc(zeros_set, 1)

            dve.wait_ge(t_ready, 1)
            dve.wait_ge(norm_consts_in, 16)
            for n, (name, lo, w) in enumerate((("w_fg", 0, D), ("w_hc", D, C))):
                dve.tensor_tensor_reduce(products[:, lo:lo + w], ps_norm[:, lo:lo + w], const(name), 1.0, 0.0,
                                         ALU.mult, ALU.add, y[:, n:n + 1]).then_inc(y_ready, 1)
            dve.wait_ge(y_ready, 2)
            dve.tensor_tensor(norm_rhs[:, :, 0:2], const("half").unsqueeze(1).to_broadcast([P, 2, 2]),
                              y[:, :].unsqueeze(2).to_broadcast([P, 2, 2]), ALU.mult).then_inc(norm_rhs_ready, 1)
            dve.wait_ge(roots_ready, 1)
            dve.reciprocal(recip_root[:, :], root[:, :]).then_inc(sigma_step, 1)
            dve.wait_ge(sigma_step, 1)
            dve.tensor_tensor(newton[:, :], squares, recip_root[:, :], ALU.mult).then_inc(sigma_step, 1)
            dve.wait_ge(sigma_step, 2)
            dve.tensor_tensor(twice_norm[:, :, :].rearrange("p n a -> p (n a)"), newton[:, :], root[:, :],
                              ALU.add).then_inc(sigma_step, 1)
            dve.wait_ge(sigma_step, 3)
            dve.reciprocal(r_y[:, :, :], twice_norm[:, :, 0:2]).then_inc(sigma_step, 1)
            dve.wait_ge(sigma_step, 4)
            dve.scalar_tensor_tensor(out=r_w[:, :, :], in0=twice_norm[:, :, 2:4], scalar=2 * EPS, in1=r_y[:, :, :],
                                     op0=ALU.add, op1=ALU.mult).then_inc(sigma_step, 1)
            dve.wait_ge(sigma_step, 5)
            dve.tensor_scalar(r_w1[:, :, :], r_w[:, :, :], EPS, 1.0, ALU.mult, ALU.add).then_inc(sigma_step, 1)
            dve.wait_ge(sigma_step, 6)
            dve.tensor_tensor(inv_sigma[:, :, :], r_w1[:, :, :], r_w[:, :, :], ALU.mult).then_inc(sigma_ready, 1)
            dve.wait_ge(sigma_ready, 1)

            def split_f(c):
                dve.wait_ge(f_hi_ready[c], 1)
                dve.scalar_tensor_tensor(out=f_parts[:, c], in0=gf_hi[:, c, 1].bitcast(F32),
                                         scalar=const("neg_second_f"), in1=gf[:, c, 1], op0=ALU.mult,
                                         op1=ALU.add).then_inc(f_ready[c], 1)

            def split_g(c):
                dve.wait_ge(g_hi_ready[c], 1)
                dve.scalar_tensor_tensor(out=g_parts[:, c], in0=gf_hi[:, c, 0].bitcast(F32),
                                         scalar=const("neg_second_g"), in1=gf[:, c, 0], op0=ALU.mult,
                                         op1=ALU.add).then_inc(g_ready[c], 1)

            dve.wait_ge(gf_ready, 1)
            dve.wait_ge(consts_in, 16)
            dve.tensor_scalar(gf[:, 0, 1], ps_st[0][:, 0:N], inv_sigma[:, 0, 0:1], const("bias_f"), ALU.mult,
                              ALU.add).then_inc(f_copied[0], 1)
            dve.wait_ge(f_copied[0], 1)
            dve.tensor_copy(gf_hi[:, 0, 1], gf[:, 0, 1]).then_inc(f_hi_ready[0], 1)
            split_f(0)
            split_g(0)

            def maxima(i):
                dve.wait_ge(scores_ready, i + 1)
                dve.tensor_reduce(row_max[:, i], ps_s[i % 2][:, :].rearrange("p (j n) -> p j n", j=J), AX_X,
                                  ALU.max).then_inc(max_ready, 1)

            def diagonal(i):
                dve.wait_ge(max_ready, i + 1)
                if i >= 2:
                    dve.wait_ge(scores_t_ready, i - 1)
                dve.tensor_tensor(max_diag[:, i % 2], ident[:, :].unsqueeze(1).to_broadcast([P, J, P]),
                                  row_max[:, i].unsqueeze(2).to_broadcast([P, J, P]), ALU.mult).then_inc(diag_ready, 1)

            def invert_sums(i):
                dve.wait_ge(out_ready, J * (i + 1))
                dve.reciprocal(r_sum[:, i], out_sums(i)).then_inc(recip_ready, 1)

            split_f(1)
            dve.wait_ge(ident_set, 1)
            maxima(0)
            for i in range(B):
                diagonal(i)
                if i + 1 < B:
                    maxima(i + 1)
                if i >= 2:
                    invert_sums(i - 2)
            dve.wait_ge(x_bias_ready, CHUNKS)

            def scale_and_add(i, j):
                dve.scalar_tensor_tensor(out=o_sb[:, i, j], in0=output(i, j)[:, 0:C], scalar=r_sum[:, i, j:j + 1],
                                         in1=x_sb[:, i // SETS, i % SETS, j], op0=ALU.mult,
                                         op1=ALU.add).then_inc(summed_last, 1)

            for i in range(BY_POOL, B):
                if i >= B - 2:
                    invert_sums(i)
                dve.wait_ge(recip_ready, i + 1)
                for j in range(J):
                    scale_and_add(i, j)

        @block.tensor
        def _(pe):
            mm = nc.tensor.matmul
            for _ in range(WARM_PRODUCTS):
                mm(ps_s[0][:, 0:256], one.to_broadcast([P, P]), one.to_broadcast([P, 256]),
                   start=True, stop=True)

            pe.wait_ge(norm_consts_in, 16)
            for lo in (0, C):
                rows = (lo, lo + C)
                for u, w, col, n in (("u_fg", "w_fg", 0, D), ("u_hc", "w_hc", D, C)):
                    last = mm(ps_norm[lo:lo + C, col:col + n], const(u, *rows).to_broadcast([C, C]), const(w, *rows),
                              start=True, stop=True)
            last.then_inc(t_ready, 1)

            def project(c):
                pe.wait_ge(xt_in[c], 16)
                for n, w in enumerate(("w_g", "w_f")):
                    for a in range(PAIRS):
                        ps = ps_st[0][:, 0:N] if (c, n) == (0, 1) else ps_gf[c][:, N * n:N * n + N]
                        last = mm(ps[2 * ROWS * a:2 * ROWS * (a + 1)], const(w), x_t[:, c, a],
                                  start=True, stop=True)
                last.then_inc(gf_ready, 1)

            def values_of(c):
                if c == 0:
                    pe.wait_ge(wv_copied, 2)
                else:
                    pe.wait_ge(sigma_step, 2)
                ps = values([ps_v, ps_norm][c])
                for a in range(PAIRS):
                    for j in range(J):
                        last = mm(ps[:, a, j].rearrange("p e f -> p (e f)"), x_t[:, c, a, P * j:P * j + P],
                                  w_v[:, :, :].rearrange("p e f -> p (e f)"), start=True, stop=True)
                last.then_inc(v_ready, 1)

            def scores(i):
                c, s = divmod(i, SETS)
                pe.wait_ge(g_ready[c], 1)
                pe.wait_ge(f_ready[c], 1)
                if i >= 2:
                    pe.wait_ge(max_ready, i - 1)
                for j in range(J):
                    last = mm(ps_s[i % 2][:, N * j:N * j + N], g_parts[set_rows(s), c, P * j:P * j + P],
                              f_parts[set_rows(s), c], start=True, stop=True)
                last.then_inc(scores_ready, 1)

            def scores_t(i):
                c, s = divmod(i, SETS)
                if i >= 2:
                    pe.wait_ge(probs_ready, i - 1)
                ps = scores_t_bank(i)
                for k in range(J):
                    mm(ps[:, k], f_parts[set_rows(s), c, P * k:P * k + P], g_parts[set_rows(s), c], start=(k == 0),
                       stop=False, skip_group_check=True)

            def subtract_maxima(i):
                pe.wait_ge(diag_ready, i + 1)
                for j in range(J):
                    last = mm(scores_t_bank(i)[:, :, P * j:P * j + P], neg_ones[:, :],
                              max_diag[:, i % 2, j].unsqueeze(1).to_broadcast([P, J, P]), start=False,
                              stop=(j == J - 1), skip_group_check=True)
                last.then_inc(scores_t_ready, 1)

            def attend(i):
                c, s = divmod(i, SETS)
                a, e = divmod(s, 2)
                pe.wait_ge(v_copied, c + 1)
                if i < 2:
                    pe.wait_ge(g_copied[i], 1)
                    pe.wait_ge(f_copied[i], 1)
                if i >= len(OUT_BANKS):
                    pe.wait_ge(scaled, i - len(OUT_BANKS) + 1)
                if i == 0:
                    pe.wait_ge(ones_set, 1)
                for j in range(J):
                    if j == 0 or i == B - 1:
                        pe.wait_ge(probs_ready, i + 1 + j)
                    for k in range(J):
                        for h in range(2):
                            at = P * j + C * h
                            last = mm(output(i, j)[C * h:C * h + C], p_t[:, i % 3, k, at:at + C],
                                      v_sb[:, c, a, k, e], start=(k == 0), stop=(k == J - 1))
                    last.then_inc(out_ready, 1)

            pe.wait_ge(norm_rhs_ready, 1)
            for n in range(2):
                last = mm(squares[:, 4 * n:4 * n + 4], y[:, n:n + 1].to_broadcast([P, P]), norm_rhs[:, n],
                          start=True, stop=True)
            last.then_inc(norms_ready, 1)
            pe.wait_ge(consts_in, 16)
            project(0)
            mm(ps_v[:, 0:C], const("w_hT", C, P), const("w_hc", C, P), start=True, stop=True).then_inc(wv_ready, 1)
            mm(bh_wc, const("b_h", C, P).to_broadcast([C, P]), const("w_hc", C, P), start=True,
               stop=True).then_inc(bh_wc_ready, 1)
            project(1)
            values_of(0)
            pe.wait_ge(zeros_set, 2)
            scores(0)
            scores(1)
            scores_t(0)
            values_of(1)
            scores(2)
            pe.wait_ge(bh_wc_scaled, 1)
            for i in range(B):
                subtract_maxima(i)
                if i >= 1:
                    attend(i - 1)
                if i + 1 < B:
                    scores_t(i + 1)
                if i + 3 < B:
                    scores(i + 3)
            attend(B - 1)


def pack_constants(Wf, bf, uf, Wg, bg, ug, Wh, bh, uh, Wc, bc, uc, gamma):
    z = np.zeros((P, NCONST), np.float32)

    def col(name):
        return z[:, COLS[name][0]:COLS[name][1]]

    col("w_fg")[:C], col("w_fg")[C:] = Wf, Wg
    col("w_hc")[:C], col("w_hc")[C:] = Wh, Wc
    col("u_fg")[:, 0] = np.concatenate([uf, ug])
    col("u_hc")[:, 0] = np.concatenate([uh, uc])
    for n, u in enumerate((uf, ug, uh, uc)):
        col("norm_rhs")[C * (n % 2):C * (n % 2) + C, 4 * (n // 2) + 2 + n % 2] = u
    col("half")[:C, 0] = 1.0
    col("half")[C:, 1] = 1.0
    col("bias_g")[:, 0] = np.tile(bg, P // D)
    col("bias_f")[:, 0] = np.tile(bf, P // D)
    part = np.arange(P) // D % BLOCKS
    col("neg_second_g")[:, 0] = np.where(part // 2 == 1, -1.0, 0.0)
    col("neg_second_f")[:, 0] = np.where(part % 2 == 1, -1.0, 0.0)
    col("gamma")[:] = gamma
    col("b_h")[C:, 0] = bh
    for e in range(2):
        rows, cols = slice(C * e, C * e + C), slice(ROWS * e, ROWS * e + ROWS)
        col("w_g")[rows, cols] = np.tile(Wg, (1, BLOCKS))
        col("w_f")[rows, cols] = np.tile(Wf, (1, BLOCKS))
        col("w_hT")[C:, C * e:C * e + C] = Wh.T
    col("b_c")[:] = bc
    return z


def kernel(**inputs):
    import numpy as _np
    import concourse.bacc as _bacc
    from concourse.bass_utils import run_bass_kernel_spmd as _run

    a = {k.replace("L0_conv_", ""): _np.asarray(v) for k, v in inputs.items()}
    x = a.pop("x")
    shape = x.shape
    xt = x.reshape(PAIRS, 2, CHUNKS, P, J, C).transpose(1, 5, 2, 0, 4, 3).reshape(P, CHUNKS, PAIRS, N)
    arrays = {"in_xt": _np.ascontiguousarray(xt), "in_x": _np.ascontiguousarray(x.reshape(B, N, C)),
              "in_consts": pack_constants(**a)}
    nc = _bacc.Bacc("TRN2", target_bir_lowering=False, num_devices=1)
    args = [nc.dram_tensor(k, v.shape, F32, kind="ExternalInput").ap() for k, v in arrays.items()]
    out = nc.dram_tensor("out", (B, N, C), F32, kind="ExternalOutput").ap()
    attention(nc, *args, out)
    r = _run(nc, [arrays], core_ids=[0])
    return r.results[0]["out"].reshape(shape)
```
